# Optimizing a Trainium2 kernel written in Bass

```python
import numpy as np
import jax
import jax.numpy as jnp

def _softmax(x, axis=-1):
    return jax.nn.softmax(x, axis=axis)

def _gelu(x):
    return jax.nn.gelu(x, approximate=True)

def _silu(x):
    return jax.nn.silu(x)

def _sigmoid(x):
    return jax.nn.sigmoid(x)

def _layernorm(x, axis=-1, eps=1e-05):
    m = jnp.mean(x, axis=axis, keepdims=True)
    v = jnp.var(x, axis=axis, keepdims=True)
    return (x - m) / jnp.sqrt(v + eps)

def _scatter_add(tgt, idx, src, axis=0):
    return tgt.at[idx].add(src)

def _segment_sum(src, seg, n):
    return jax.ops.segment_sum(src, seg, n)
kernel_name = 'mk_flamingo_gated_d1_seqx_r4_f2d1d1'

def setup_inputs(seed: int=0):
    np.random.seed(seed)
    _w = jnp.asarray

    def _rec_inputs():
        import jax
        import jax.numpy as jnp
        _rk = jax.random.key(seed)
        x = -0.0002928 + 1 * jax.random.normal(jax.random.fold_in(_rk, 1), (8, 512, 256), jnp.float32)
        _lenS = 512 - jax.random.randint(jax.random.fold_in(_rk, 7), (8,), 0, max(1, 512 // 4) + 1, jnp.int32)
        _lenS2 = 1024 - jax.random.randint(jax.random.fold_in(_rk, 8), (8,), 0, max(1, 1024 // 4) + 1, jnp.int32)
        _ctx_1024P = jax.random.normal(jax.random.fold_in(_rk, 11), (8, 16, 256), jnp.float32)
        _ctx_1024c = jax.random.dirichlet(jax.random.fold_in(_rk, 511), 0.3 * jnp.ones((16,), jnp.float32), (8, 1024))
        _ctx_1024t = jnp.einsum('bsk,bkd->bsd', _ctx_1024c, _ctx_1024P)
        _ctx_1024t = _ctx_1024t * jax.lax.rsqrt(jnp.mean(jnp.square(_ctx_1024t)) + 1e-12) * 0.953939
        ctx_1024 = -1.39393e-06 + 0.999914 * (_ctx_1024t + 0.3 * jax.random.normal(jax.random.fold_in(_rk, 611), (8, 1024, 256), jnp.float32))
        _validS = jnp.arange(512)[None, :] < _lenS[:, None]
        _validS2 = jnp.arange(1024)[None, :] < _lenS2[:, None]
        _causal = jnp.tril(jnp.ones((512, 512), dtype=bool))
        mask_BxSxS2_if1 = jnp.where(jnp.ones((8, 512, 1024), dtype=bool), 1, 0).astype(jnp.int32)
        _g = jax.random.normal(jax.random.fold_in(_rk, 9001), (2, 1), jnp.float32)
        _g = jnp.sign(_g) * jnp.maximum(jnp.abs(_g), 1.0) + (_g == 0) * 1.0
        g_xattn = _g[0]
        g_ffn = _g[1]
        return (x, ctx_1024, mask_BxSxS2_if1, g_xattn, g_ffn)
    x, ctx_1024, mask_BxSxS2_if1, g_xattn, g_ffn = _rec_inputs()

    def _L0_xattn_setup():
        import jax, jax.numpy as jnp
        import numpy as np
        B, S, D, H = (2, 512, 256, 16)
        DK = D // H
        K = 32
        NEG = -1000000000.0
        rng = jax.random.key(seed)
        ks = jax.random.split(rng, 12)

        def w(k):
            return jax.random.normal(k, (D, D), jnp.float32) * 0.02

        def b(k):
            return jax.random.normal(k, (D,), jnp.float32) * 0.02
        return {'query': jax.random.normal(ks[0], (B, S, D), jnp.float32), 'key': jax.random.normal(ks[1], (B, S, D), jnp.float32), 'value': jax.random.normal(ks[2], (B, S, D), jnp.float32), 'Wq': w(ks[3]), 'bq': b(ks[4]), 'Wk': w(ks[5]), 'bk': b(ks[6]), 'Wv': w(ks[7]), 'bv': b(ks[8]), 'Wo': w(ks[9]), 'bo': b(ks[10]), 'mask': jnp.ones((B, S, S), jnp.int32), 'topk': K}
    _L0_xattn_all = _L0_xattn_setup()
    _L0_xattn_in = {k: v for k, v in _L0_xattn_all.items() if k in ('Wq', 'bq', 'Wk', 'bk', 'Wv', 'bv', 'Wo', 'bo')}
    del _L0_xattn_all

    def _L0_ffn_setup():
        import jax, jax.numpy as jnp
        import numpy as np
        TOP_K = 2
        CAPACITY_FACTOR = 1.25

        def _moe_forward(x, gate_w, wi_gate, wi_up, wo):
            B, S, D = x.shape
            E = wi_gate.shape[0]
            N = B * S
            capacity = max(int(N / E * CAPACITY_FACTOR), 1)
            x_flat = x.reshape(N, D)
            router_logits = x_flat @ gate_w.T
            router_probs = jax.nn.softmax(router_logits, axis=-1)
            top_k_probs, top_k_idx = jax.lax.top_k(router_probs, TOP_K)
            top_k_probs = top_k_probs / jnp.sum(top_k_probs, axis=-1, keepdims=True)
            out = jnp.zeros_like(x_flat)
            experts = jnp.arange(E, dtype=jnp.int32)
            for k in range(TOP_K):
                eid = top_k_idx[:, k]
                ew = top_k_probs[:, k]
                onehot = (eid[:, None] == experts[None, :]).astype(jnp.int32)
                pos_all = jnp.cumsum(onehot, axis=0) - 1
                pos = jnp.take_along_axis(pos_all, eid[:, None].astype(jnp.int32), axis=1)[:, 0]
                valid = pos < capacity
                pos_c = jnp.where(valid, pos, 0)
                disp = jnp.zeros((E, capacity, D), x_flat.dtype).at[eid, pos_c].add(jnp.where(valid[:, None], x_flat, 0.0))
                gate = jax.nn.silu(jnp.einsum('ecd,efd->ecf', disp, wi_gate))
                up = jnp.einsum('ecd,efd->ecf', disp, wi_up)
                expert_out = jnp.einsum('ecf,edf->ecd', gate * up, wo)
                tok_out = expert_out[eid, pos_c]
                out = out + jnp.where(valid[:, None], ew[:, None] * tok_out, 0.0)
            return out.reshape(B, S, D)
        key = jax.random.key(seed)
        k1, k2, k3, k4, k5 = jax.random.split(key, 5)
        B, S, D, F, E = (4, 512, 256, 1024, 8)
        return {'x': jax.random.normal(k1, (B, S, D), dtype=jnp.float32), 'gate_w': jax.random.normal(k2, (E, D), dtype=jnp.float32) * 0.02, 'wi_gate': jax.random.normal(k3, (E, F, D), dtype=jnp.float32) * 0.02, 'wi_up': jax.random.normal(k4, (E, F, D), dtype=jnp.float32) * 0.02, 'wo': jax.random.normal(k5, (E, D, F), dtype=jnp.float32) * 0.02}
    _L0_ffn_all = _L0_ffn_setup()
    _L0_ffn_in = {k: v for k, v in _L0_ffn_all.items() if k in ('gate_w', 'wi_gate', 'wi_up', 'wo')}
    del _L0_ffn_all
    return {'x': x, 'ctx_1024': ctx_1024, 'mask_BxSxS2_if1': mask_BxSxS2_if1, 'g_xattn': g_xattn, 'g_ffn': g_ffn, 'L0_xattn_Wq': _L0_xattn_in['Wq'], 'L0_xattn_bq': _L0_xattn_in['bq'], 'L0_xattn_Wk': _L0_xattn_in['Wk'], 'L0_xattn_bk': _L0_xattn_in['bk'], 'L0_xattn_Wv': _L0_xattn_in['Wv'], 'L0_xattn_bv': _L0_xattn_in['bv'], 'L0_xattn_Wo': _L0_xattn_in['Wo'], 'L0_xattn_bo': _L0_xattn_in['bo'], 'L0_ffn_gate_w': _L0_ffn_in['gate_w'], 'L0_ffn_wi_gate': _L0_ffn_in['wi_gate'], 'L0_ffn_wi_up': _L0_ffn_in['wi_up'], 'L0_ffn_wo': _L0_ffn_in['wo']}

def reference(x, ctx_1024, mask_BxSxS2_if1, g_xattn, g_ffn, L0_xattn_Wq, L0_xattn_bq, L0_xattn_Wk, L0_xattn_bk, L0_xattn_Wv, L0_xattn_bv, L0_xattn_Wo, L0_xattn_bo, L0_ffn_gate_w, L0_ffn_wi_gate, L0_ffn_wi_up, L0_ffn_wo):
    import jax
    import jax.numpy as jnp

    def _L0_xattn_ref(query, key, value, Wq, bq, Wk, bk, Wv, bv, Wo, bo, mask, topk):
        import jax, jax.numpy as jnp
        import numpy as np
        B, S, D, H = (2, 512, 256, 16)
        DK = D // H
        K = 32
        NEG = -1000000000.0
        Bn, Sq, Dm = query.shape
        q = (query @ Wq.T + bq).reshape(Bn, Sq, H, DK).transpose(0, 2, 1, 3)
        k = (key @ Wk.T + bk).reshape(Bn, -1, H, DK).transpose(0, 2, 1, 3)
        v = (value @ Wv.T + bv).reshape(Bn, -1, H, DK).transpose(0, 2, 1, 3)
        scores = jnp.einsum('bhqd,bhkd->bhqk', q, k) / jnp.asarray(np.sqrt(DK), (scores_dtype := q.dtype))
        scores = jnp.where(mask[:, None] == 0, jnp.asarray(NEG, scores.dtype), scores)
        kk = min(topk, scores.shape[-1])
        vals, idx = jax.lax.top_k(scores, kk)
        p = jax.nn.softmax(vals, axis=-1)
        vg = jnp.take_along_axis(v[:, :, None, :, :], idx[..., None], axis=3)
        ctx = jnp.einsum('bhqk,bhqkd->bhqd', p, vg)
        x = ctx.transpose(0, 2, 1, 3).reshape(Bn, Sq, Dm)
        return x @ Wo.T + bo

    def _L0_ffn_ref(x, gate_w, wi_gate, wi_up, wo):
        import jax, jax.numpy as jnp
        import numpy as np
        TOP_K = 2
        CAPACITY_FACTOR = 1.25

        def _moe_forward(x, gate_w, wi_gate, wi_up, wo):
            B, S, D = x.shape
            E = wi_gate.shape[0]
            N = B * S
            capacity = max(int(N / E * CAPACITY_FACTOR), 1)
            x_flat = x.reshape(N, D)
            router_logits = x_flat @ gate_w.T
            router_probs = jax.nn.softmax(router_logits, axis=-1)
            top_k_probs, top_k_idx = jax.lax.top_k(router_probs, TOP_K)
            top_k_probs = top_k_probs / jnp.sum(top_k_probs, axis=-1, keepdims=True)
            out = jnp.zeros_like(x_flat)
            experts = jnp.arange(E, dtype=jnp.int32)
            for k in range(TOP_K):
                eid = top_k_idx[:, k]
                ew = top_k_probs[:, k]
                onehot = (eid[:, None] == experts[None, :]).astype(jnp.int32)
                pos_all = jnp.cumsum(onehot, axis=0) - 1
                pos = jnp.take_along_axis(pos_all, eid[:, None].astype(jnp.int32), axis=1)[:, 0]
                valid = pos < capacity
                pos_c = jnp.where(valid, pos, 0)
                disp = jnp.zeros((E, capacity, D), x_flat.dtype).at[eid, pos_c].add(jnp.where(valid[:, None], x_flat, 0.0))
                gate = jax.nn.silu(jnp.einsum('ecd,efd->ecf', disp, wi_gate))
                up = jnp.einsum('ecd,efd->ecf', disp, wi_up)
                expert_out = jnp.einsum('ecf,edf->ecd', gate * up, wo)
                tok_out = expert_out[eid, pos_c]
                out = out + jnp.where(valid[:, None], ew[:, None] * tok_out, 0.0)
            return out.reshape(B, S, D)
        return _moe_forward(x, gate_w, wi_gate, wi_up, wo)
    x = x + jnp.tanh(g_xattn[0]) * _L0_xattn_ref(_layernorm(x, axis=-1), ctx_1024, ctx_1024, L0_xattn_Wq, L0_xattn_bq, L0_xattn_Wk, L0_xattn_bk, L0_xattn_Wv, L0_xattn_bv, L0_xattn_Wo, L0_xattn_bo, mask_BxSxS2_if1, 32)
    x = x + jnp.tanh(g_ffn[0]) * _L0_ffn_ref(_layernorm(x, axis=-1), L0_ffn_gate_w, L0_ffn_wi_gate, L0_ffn_wi_up, L0_ffn_wo)
    return x

_drawn_inputs = setup_inputs


def setup_inputs(seed=0):
    import zlib

    import numpy as np

    out = dict(_drawn_inputs(seed))
    spreads = {}
    factors = {'L0_xattn_bq': 8.0,
     'L0_xattn_bk': 64.0,
     'L0_xattn_bv': 8.0,
     'L0_xattn_bo': 3.574,
     'L0_ffn_gate_w': 7.76}
    for name, (base, spread) in spreads.items():
        noise = np.random.default_rng([zlib.crc32(name.encode()), seed]).standard_normal(out[name].shape)
        drawn = base * np.exp(spread * noise) if base else spread * noise
        out[name] = jnp.asarray(drawn.astype(out[name].dtype))
    for name, factor in factors.items():
        out[name] = (out[name] * factor).astype(out[name].dtype)
    return out
```

```python
from contextlib import ExitStack

import concourse.bass as bass
from concourse import mybir

F32 = mybir.dt.float32
F32R = mybir.dt.float32r
BF16 = mybir.dt.bfloat16
I32 = mybir.dt.int32
U32 = mybir.dt.uint32
ALU = mybir.AluOpType
ACT = mybir.ActivationFunctionType
AX_X = mybir.AxisListType.X

P = 128
LN_EPS = 1e-5
NEG = -1.0e9
TAKEN = -3.0e38


class Plan:

    def __init__(self, B, S, S2, D, E, F, H=16, topk=32):
        self.B, self.S, self.S2, self.D, self.E, self.F, self.H = B, S, S2, D, E, F, H
        self.DK = D // H
        self.HG = 4
        self.G = H // self.HG
        self.QT = S // P
        self.KB = S2 // P
        self.KD = D // P
        self.TERMS = 6
        self.KR = self.TERMS * self.DK
        self.q_spans = [(0, 0, 1), (1, 0, 1), (2, 0, 1), (3, 1, 1), (4, 1, 1), (5, 2, 1)]
        self.k_spans = [(0, 0, 3), (3, 0, 2), (5, 0, 1)]
        self.VW = 32
        self.TILES = self.QT * self.HG
        self.ITER = B * self.G
        self.TT = B * self.QT
        self.TOPK = topk
        self.ROUNDS = topk // 8
        self.CH = 24
        self.cut = [S2 * c // self.CH for c in range(self.CH + 1)]
        self.RA = 3
        self.NA = self.RA * self.CH
        self.NC = 8 + 8 * self.CH
        N = B * S
        self.N = N
        self.CAP = max(int(N / E * 1.25), 1)


def over(eng, total, step, body):
    for u in range(step):
        body(u, u, True)
    if total > step:
        with eng.Fori(1, total // step) as r:
            for u in range(step):
                body(r * step + u, u, False)


def project(nc, pl, io, scr):
    QT, KB, KD, S, S2, D = pl.QT, pl.KB, pl.KD, pl.S, pl.S2, pl.D
    NH = S2 // 512
    with ExitStack() as ctx:
        sb = lambda name, shape, dt=F32: ctx.enter_context(nc.sbuf_tensor(name, shape, dt))
        psum = lambda name: ctx.enter_context(nc.psum_tensor(name, [P, 512], F32))
        sem = lambda name: ctx.enter_context(nc.semaphore(name))

        wq, wk, wv = (sb(n, [P, KD, D]) for n in ("p_wq", "p_wk", "p_wv"))
        bq, bk = (sb(n, [P, KD]) for n in ("p_bq", "p_bk"))
        bqs = sb("p_bqs", [P, KD])
        bv = sb("p_bv", [P, D])
        ident = sb("p_ident", [P, P])
        xin = sb("p_xin", [P, 2, QT, D])
        ctxT = sb("p_ctxT", [P, 2, KD, S2])
        stats = sb("p_stats", [P, 2, QT, 6])
        mv = sb("p_mv", [P, 2, QT, 2])
        veps = sb("p_veps", [P, 2, QT])
        std = sb("p_std", [P, 2, QT])
        rstd = sb("p_rstd", [P, 2, QT])
        xn = sb("p_xn", [P, 2, QT, D])
        xnT = sb("p_xnT", [P, KD, S])
        qf = sb("p_qf", [P, 2, KD, S])
        kf = sb("p_kf", [P, 2, KD, S2])
        qp = sb("p_qp", [P, 2, 3, KD, S], BF16)
        kp = sb("p_kp", [P, 2, 3, KD, S2], BF16)
        vp = sb("p_vp", [P, 2, KB, pl.H, pl.VW])
        ring_a = [psum(f"p_ra{i}") for i in range(4)]
        ring_v = [psum(f"p_rv{i}") for i in range(4)]

        w_in = sem("p_w_in")
        x_in = [sem(f"p_x_in{u}") for u in range(2)]
        c_in = [sem(f"p_c_in{u}") for u in range(2)]
        const_ready = sem("p_const")
        bqs_ready = sem("p_bqs_ready")
        id0 = sem("p_id0")
        ln_stats = sem("p_ln_stats")
        ln_std = sem("p_ln_std")
        xn_ready = sem("p_xn_ready")
        a_full = sem("p_a_full")
        a_used = sem("p_a_used")
        v_full = sem("p_v_full")
        v_used = sem("p_v_used")
        q_split = sem("p_q_split")
        k_split = sem("p_k_split")
        stored = [sem(f"p_stored{u}") for u in range(2)]
        own = sem("p_own")
        AF = KD + KD + KD * NH
        VF = KB // 2
        STORES = 2 * 3 * KD + pl.G
        block = ctx.enter_context(nc.Block())

        @block.sync
        def _(sp):
            for dst, src in ((wq, io["wqT"]), (wk, io["wkT"]), (wv, io["wvT"])):
                sp.dma_start(dst[:], src.rearrange("(k p) n -> p k n", p=P)).then_inc(w_in, 16)
            for dst, src in ((bq, io["bq"]), (bk, io["bk"])):
                sp.dma_start(dst[:], src).then_inc(w_in, 16)
            sp.dma_start(bv[:], io["bv"].partition_broadcast(P)).then_inc(w_in, 16)

            def store(n, u, first):
                sp.wait_ge(k_split, n + 1)
                for i in range(3):
                    for m in range(KD):
                        sp.dma_start(scr["k"][n, 2 * m:2 * m + 2, i * 64:(i + 1) * 64, :], kp[:, u, i, m, :]
                                     ).then_inc(stored[u], 16)
                for g in range(pl.G):
                    sp.dma_start(scr["v"][n, g], vp[:, u, :, 4 * g:4 * g + 4, :].rearrange("p k h c -> p k (h c)")
                                   ).then_inc(stored[u], 16)
                sp.wait_ge(q_split, n + 1)
                for i in range(3):
                    for m in range(KD):
                        sp.dma_start(scr["q"][n, 2 * m:2 * m + 2, i * 64:(i + 1) * 64, :], qp[:, u, i, m, :]
                                     ).then_inc(stored[u], 16)

            over(sp, pl.B, 2, store)
            for u in range(2):
                sp.wait_ge(stored[u], 16 * STORES * (pl.B // 2))

        @block.gpsimd
        def _(pool):
            nc.gpsimd.memset(ident[:], 0.0).then_inc(id0, 1)
            nc.gpsimd.memset(vp[:], 0.0).then_inc(id0, 1)
            pool.wait_ge(id0, 2)
            nc.gpsimd.affine_select(out=ident[:], in_=ident[:], compare_op=ALU.not_equal, fill=1.0, base=0,
                                    pattern=[[-1, P]], channel_multiplier=1).then_inc(const_ready, 1)
            nc.gpsimd.memset(vp[:, :, :, :, pl.DK:pl.DK + 1], 1.0).then_inc(const_ready, 1)

            def load(n, u, first):
                if not first:
                    pool.wait_ge(xn_ready, n - 1)
                pool.dma_start(xin[:, u], io["x"][n].rearrange("(t p) d -> p t d", p=P)).then_inc(x_in[u], 16)
                if not first:
                    pool.wait_ge(a_full, (n - 1) * AF)
                pool.dma_start(ctxT[:, u], io["ctxT"][n].rearrange("(k p) s -> p k s", p=P)).then_inc(c_in[u], 16)

            over(pool, pl.B, 2, load)

        @block.tensor
        def _(pe):
            pe.wait_ge(w_in, 16 * 6)
            pe.wait_ge(const_ready, 1)

            def batch(n, u, first):
                pe.wait_ge(c_in[u], 16 * (n // 2 + 1) if first else (n - u) * 8 + 16)
                for f in range(VF):
                    if not (first and n == 0):
                        pe.wait_ge(v_used, n * VF + f - 3)
                    for i in range(2):
                        for k in range(KD):
                            mm = nc.tensor.matmul(ring_v[f % 4][:, i * D:(i + 1) * D],
                                                  ctxT[:, u, k, (2 * f + i) * P:(2 * f + i + 1) * P], wv[:, k, :],
                                                  start=(k == 0), stop=(k == KD - 1))
                    mm.then_inc(v_full, 1)
                f = 0
                for m in range(KD):
                    for h in range(NH):
                        if not (first and n == 0):
                            pe.wait_ge(a_used, n * AF + f - 3)
                        for k in range(KD):
                            mm = nc.tensor.matmul(ring_a[f % 4][:, :], wk[:, k, m * P:(m + 1) * P],
                                                  ctxT[:, u, k, h * 512:(h + 1) * 512], start=(k == 0), stop=(k == KD - 1))
                        mm.then_inc(a_full, 1)
                        f += 1
                pe.wait_ge(xn_ready, n + 1)
                for k in range(KD):
                    pe.wait_ge(a_used, n * AF + f - 3)
                    for t in range(QT):
                        mm = nc.tensor.transpose(ring_a[f % 4][:, t * P:(t + 1) * P], xn[:, u, t, k * P:(k + 1) * P], ident[:])
                    mm.then_inc(a_full, 1)
                    f += 1
                pe.wait_ge(a_used, n * AF + f)
                for m in range(KD):
                    for k in range(KD):
                        mm = nc.tensor.matmul(ring_a[f % 4][:, 0:S], wq[:, k, m * P:(m + 1) * P], xnT[:, k, :],
                                              start=(k == 0), stop=(k == KD - 1))
                    mm.then_inc(a_full, 1)
                    f += 1

            over(pe, pl.B, 2, batch)

        @block.scalar
        def _(act):
            act.wait_ge(w_in, 16 * 6)
            act.wait_ge(bqs_ready, 1)

            def batch(n, u, first):
                act.wait_ge(ln_stats, n + 1)
                nc.scalar.activation(std[:, u], veps[:, u], ACT.Sqrt).then_inc(ln_std, 1)
                f = 0
                if not first:
                    act.wait_ge(k_split, n - 1)
                for m in range(KD):
                    for h in range(NH):
                        act.wait_ge(a_full, n * AF + f + 1)
                        nc.scalar.activation(kf[:, u, m, h * 512:(h + 1) * 512], ring_a[f % 4][:], ACT.Identity,
                                             bias=bk[:, m:m + 1]).then_inc(a_used, 1)
                        f += 1
                for k in range(KD):
                    act.wait_ge(a_full, n * AF + f + 1)
                    nc.scalar.copy(xnT[:, k, :], ring_a[f % 4][:, 0:S]).then_inc(a_used, 1)
                    f += 1
                if not first:
                    act.wait_ge(q_split, n - 1)
                for m in range(KD):
                    act.wait_ge(a_full, n * AF + f + 1)
                    nc.scalar.activation(qf[:, u, m, :], ring_a[f % 4][:, 0:S], ACT.Identity,
                                         bias=bqs[:, m:m + 1], scale=float(pl.DK) ** -0.5).then_inc(a_used, 1)
                    f += 1

            over(act, pl.B, 2, batch)

        @block.vector
        def _(dve):
            dve.wait_ge(w_in, 16 * 6)
            nc.vector.tensor_scalar(bqs[:], bq[:], float(pl.DK) ** -0.5, None, ALU.mult).then_inc(bqs_ready, 1)
            dve.wait_ge(const_ready, 2)

            def batch(n, u, first):
                done = [0]

                def link(ins):
                    done[0] += 1
                    ins.then_inc(own, 1)
                    dve.wait_ge(own, done[0])

                dve.wait_ge(x_in[u], 16 if first else (n - u) * 8 + 16)
                for t in range(QT):
                    ins = nc.vector.bn_stats(stats[:, u, t, :], xin[:, u, t, :])
                link(ins)
                for t in range(QT):
                    ins = nc.vector.bn_aggr(mv[:, u, t, :], stats[:, u, t, :])
                link(ins)
                nc.vector.tensor_scalar(veps[:, u], mv[:, u, :, 1], LN_EPS, None, ALU.add).then_inc(ln_stats, 1)
                for f in range(VF):
                    dve.wait_ge(v_full, n * VF + f + 1)
                    if f == 0 and not first:
                        dve.wait_ge(stored[u], (n - u) * (8 * STORES))
                    nc.vector.tensor_tensor(
                        vp[:, u, 2 * f:2 * f + 2, :, 0:pl.DK],
                        ring_v[f % 4][:, :].rearrange("p (i h d) -> p i h d", i=2, h=pl.H),
                        bv[:].rearrange("p (h d) -> p h d", h=pl.H).unsqueeze(1).broadcast_to([P, 2, pl.H, pl.DK]),
                        ALU.add).then_inc(v_used, 1)
                dve.wait_ge(ln_std, n + 1)
                link(nc.vector.reciprocal(rstd[:, u], std[:, u]))
                if not first:
                    dve.wait_ge(a_full, n * AF - KD)
                for t in range(QT):
                    ins = nc.vector.tensor_scalar(xn[:, u, t, :], xin[:, u, t, :], mv[:, u, t, 0:1], rstd[:, u, t:t + 1],
                                                  ALU.subtract, ALU.mult)
                ins.then_inc(xn_ready, 1)
                for whole, parts, fills, sem_split in (
                        (kf, kp, KD * NH, k_split), (qf, qp, AF, q_split)):
                    dve.wait_ge(a_used, n * AF + fills)
                    w, p1, p2, p3 = whole[:, u], parts[:, u, 0], parts[:, u, 1], parts[:, u, 2]
                    link(nc.vector.tensor_copy(p1, w))
                    link(nc.vector.tensor_tensor(w, w, p1, ALU.subtract))
                    link(nc.vector.tensor_copy(p2, w))
                    nc.vector.tensor_tensor(p3, w, p2, ALU.subtract).then_inc(sem_split, 1)
                dve.wait_ge(own, done[0])
                dve.wait_ge(q_split, n + 1)
                nc.vector.sem_clear(own)

            over(dve, pl.B, 2, batch)


def attend(nc, pl, io, scr, keep):
    G, TILES, KB, HG, DK, VW, KR, S, S2 = pl.G, pl.TILES, pl.KB, pl.HG, pl.DK, pl.VW, pl.KR, pl.S, pl.S2
    GI = TILES // HG
    CH, NA, NC = pl.CH, pl.NA, pl.NC
    assert pl.TT == pl.ITER
    LAG = 4
    with ExitStack() as ctx:
        sb = lambda name, shape, dt=F32: ctx.enter_context(nc.sbuf_tensor(name, shape, dt))
        psum = lambda name, cols=512: ctx.enter_context(nc.psum_tensor(name, [P, cols], F32))
        sem = lambda name: ctx.enter_context(nc.semaphore(name))

        qs = sb("a_qs", [KR, 2, HG, S], BF16)
        ks = sb("a_ks", [KR, 2, HG, S2], BF16)
        vs = sb("a_vs", [P, 2, KB, HG * VW])
        ident = sb("a_ident", [P, P])
        sc = sb("a_sc", [P, 4, S2])
        low = sb("a_low", [P, 2, S2], BF16)
        ex = sb("a_ex", [P, 2, S2])
        exT = sb("a_exT", [P, 8, S2])
        cand = sb("a_cand", [P, 2, TILES, NC])
        work = sb("a_work", [P, 2, 8 + NA])
        top = sb("a_top", [P, 2, TILES, pl.TOPK])
        nmax = sb("a_nmax", [P, 2, TILES])
        lowest = sb("a_lowest", [P, P], BF16)
        outT = sb("a_outT", [P, 2, P])
        zeros = sb("a_zeros", [P, scr["disp_z"].shape[2]])
        rden = sb("a_rden", [P, 2, HG])
        row_of = sb("a_row_of", [P, TILES, TILES], BF16)
        mask = sb("a_mask", [P, 2, S2], I32)
        square = sb("a_square", [P, S2])
        sign = sb("a_sign", [P, S2], BF16)
        counts = sb("a_counts", [TILES, 512])
        attn, lows, nonzero = keep["attn"], keep["lows"], keep["nonzero"]
        ps_s = psum("a_ps_s", S2)
        ps_e = psum("a_ps_e", S2)
        ps_t = [psum(f"a_ps_t{i}") for i in range(2)]
        ps_ou = psum("a_ps_ou")
        ps_c = psum("a_ps_c")

        id0 = sem("a_id0")
        zeroed = sem("a_zeroed")
        ident_ready = sem("a_ident_ready")
        loaded = [sem(f"a_loaded{u}") for u in range(2)]
        mask_in = [sem(f"a_mask_in{u}") for u in range(2)]
        squared = sem("a_squared")
        mask_seen = sem("a_mask_seen")
        scored = sem("a_scored")
        copied = [sem(f"a_copied{u}") for u in range(2)]
        own = sem("a_own")
        thresh = sem("a_thresh")
        lowed = sem("a_lowed")
        masked = sem("a_masked")
        expd = sem("a_expd")
        turned = sem("a_turned")
        turned_sb = sem("a_turned_sb")
        pv_done = sem("a_pv_done")
        out_sb = sem("a_out_sb")
        out_turned = sem("a_out_turned")
        recip = sem("a_recip")
        normed = sem("a_normed")
        counted = sem("a_counted")
        summed = sem("a_summed")
        LOADS = len(pl.q_spans) + len(pl.k_spans) + 1
        block = ctx.enter_context(nc.Block())

        @block.sync
        def _(sp):
            def load(I, u, first):
                if not first:
                    sp.wait_ge(pv_done, GI * (I - 1))
                for dst, src, spans in ((ks, scr["k"][I], pl.k_spans), (qs, scr["q"][I], pl.q_spans)):
                    parts = src.rearrange("(r j) n -> r j n", j=HG)
                    for term, part, n in spans:
                        sp.dma_start(dst[term * DK:(term + n) * DK, u], parts[part * DK:(part + n) * DK]
                                     ).then_inc(loaded[u], 16)
                sp.dma_start(vs[:, u], scr["v"][I]).then_inc(loaded[u], 16)
                if not first:
                    sp.wait_ge(squared, I - 1)
                sp.dma_start(mask[:, u], mask_tiles[I]).then_inc(mask_in[u], 16)
                sp.dma_start(scr["disp_z"][I], zeros[:]).then_inc(zeroed, 16)

            sp.wait_ge(id0, 3)
            mask_tiles = io["mask"].rearrange("b (t p) s -> (b t) p s", p=P)
            over(sp, pl.ITER, 2, load)
            sp.wait_ge(zeroed, 16 * pl.ITER)

        @block.tensor
        def _(pe):
            pe.wait_ge(ident_ready, 2 + TILES)

            def scores(T, i, u, fresh):
                j, qt = i % HG, i // HG
                if i:
                    pe.wait_ge(copied[u], i)
                elif not fresh:
                    pe.wait_ge(copied[1 - u], TILES)
                for h in range(S2 // 512):
                    mm = nc.tensor.matmul(ps_s[:, h * 512:(h + 1) * 512], qs[:, u, j, qt * P:(qt + 1) * P],
                                          ks[:, u, j, h * 512:(h + 1) * 512], start=True, stop=True)
                mm.then_inc(scored, 1)

            def mark(T, i, u, fresh):
                j, qt = i % HG, i // HG
                if not fresh:
                    pe.wait_ge(expd, T)
                for h in range(S2 // 512):
                    half = slice(h * 512, (h + 1) * 512)
                    nc.tensor.matmul(ps_e[:, half], qs[:, u, j, qt * P:(qt + 1) * P], ks[:, u, j, half],
                                     start=True, stop=False)
                    mm = nc.tensor.matmul(ps_e[:, half], lowest[:], low[:, i % 2, half], start=False, stop=True)
                mm.then_inc(masked, 1)

            def count(I, T, i, fresh):
                if i == 0 and not fresh:
                    pe.wait_ge(summed, I)
                pe.wait_ge(lowed, T + 1)
                for h in range(S2 // 512):
                    mm = nc.tensor.matmul(ps_c[0:TILES, :], row_of[:, i, :], low[:, i % 2, h * 512:(h + 1) * 512],
                                          start=(i == 0 and h == 0), stop=(i == TILES - 1 and h == S2 // 512 - 1))
                if i == TILES - 1:
                    mm.then_inc(counted, 1)

            def turn(T, i, fresh):
                pe.wait_ge(expd, T + 1)
                for h in range(2):
                    if not fresh:
                        pe.wait_ge(turned_sb, 2 * T + h - 1)
                    for c in range(KB // 2):
                        k = KB // 2 * h + c
                        mm = nc.tensor.transpose(ps_t[h][:, c * P:(c + 1) * P], ex[:, i % 2, k * P:(k + 1) * P],
                                                 ident[:])
                    mm.then_inc(turned, 1)

            def values(Gn, gi, u, fresh):
                pe.wait_ge(turned_sb, 2 * HG * Gn + 2 * HG)
                if not fresh:
                    pe.wait_ge(normed, Gn)
                for k in range(KB):
                    for j in range(HG):
                        mm = nc.tensor.matmul(ps_ou[VW * j:VW * (j + 1), 0:P], vs[:, u, k, VW * j:VW * (j + 1)],
                                              exT[:, HG * (gi % 2) + j, k * P:(k + 1) * P],
                                              start=(k == 0), stop=(k == KB - 1), tile_position=(0, VW * j))
                mm.then_inc(pv_done, 1)

            def turn_out(Gn, gi, fresh):
                pe.wait_ge(out_sb, Gn + 1)
                nc.tensor.transpose(ps_ou[:, P:2 * P], outT[:, gi % 2, :], ident[:]).then_inc(out_turned, 1)

            def step(I, i, u, start):
                if i < TILES:
                    scores(I * TILES + i, i, u, start and i < 1)
                t = i - LAG
                if t < TILES and not (start and t < 0):
                    count(I, I * TILES + t, t % TILES, start)
                    mark(I * TILES + t, t % TILES, u if t >= 0 else 1 - u, start and t == 0)
                t = i - LAG - 1
                if t < TILES and not (start and t < 0):
                    turn(I * TILES + t, t % TILES, start and t == 0)
                d = (i - LAG - 5) // HG
                if (i - LAG - 5) % HG == 0 and d < GI and not (start and d < 0):
                    values(I * GI + d, d % GI, u if d >= 0 else 1 - u, start and d == 0)
                d = (i - LAG - 7) // HG
                if (i - LAG - 7) % HG == 0 and d < GI and not (start and d < 0):
                    turn_out(I * GI + d, d % GI, start and d == 0)

            def iteration(I, u, first):
                pe.wait_ge(loaded[u], 16 * LOADS if first else (I - u) * (8 * LOADS) + 16 * LOADS)
                for i in range(TILES):
                    step(I, i, u, first and u == 0)

            over(pe, pl.ITER, 2, iteration)
            for i in range(TILES, TILES + LAG + 5):
                step(pl.ITER - 1, i, 1, False)

        @block.scalar
        def _(act):
            def take_out(Gn, gi, start):
                act.wait_ge(pv_done, Gn + 1)
                if not (start and gi < 2):
                    act.wait_ge(out_turned, Gn - 1)
                nc.scalar.copy(outT[:, gi % 2, :], ps_ou[:, 0:P]).then_inc(out_sb, 1)

            def normalise(Gn, gi):
                act.wait_ge(recip, Gn + 1)
                for j in range(HG):
                    ins = nc.scalar.activation(attn[:, bass.ds(Gn, 1), j * DK:(j + 1) * DK].rearrange("p o d -> p (o d)"),
                                               ps_ou[:, P + j * VW:P + j * VW + DK], ACT.Identity,
                                               scale=rden[:, gi % 2, j:j + 1])
                ins.then_inc(normed, 1)

            def step(I, i, u, start):
                T = I * TILES + i
                if i < TILES:
                    act.wait_ge(scored, T + 1)
                    if not (start and i < 4):
                        act.wait_ge(lowed, T - 3)
                    nc.scalar.copy(sc[:, i % 4, :], ps_s[:]).then_inc(copied[u], 1)
                t = i - LAG
                if t < TILES and not (start and t < 0):
                    s, v = t % TILES, u if t >= 0 else 1 - u
                    act.wait_ge(masked, T - LAG + 1)
                    if not (start and t < 2):
                        act.wait_ge(turned, 2 * (T - LAG) - 2)
                    nc.scalar.activation(ex[:, s % 2, :], ps_e[:], ACT.Exp, bias=nmax[:, v, s:s + 1]).then_inc(expd, 1)
                t = i - LAG - 1
                if t < TILES and not (start and t < 0):
                    if t % HG == 0 and not (start and t < 8):
                        act.wait_ge(pv_done, I * GI + t // HG - 1)
                    for h in range(2):
                        act.wait_ge(turned, 2 * (T - LAG) - 1 + h)
                        nc.scalar.copy(exT[:, t % 8, h * 512:(h + 1) * 512], ps_t[h][:]).then_inc(turned_sb, 1)
                d = (i - LAG - 6) // HG
                if (i - LAG - 6) % HG == 0 and d < GI and not (start and d < 0):
                    take_out(I * GI + d, d % GI, start)
                d = (i - LAG - 8) // HG
                if (i - LAG - 8) % HG == 0 and d < GI and not (start and d < 0):
                    normalise(I * GI + d, d % GI)

            def count_mask(I, u, i, first):
                if i == 5:
                    act.wait_ge(mask_in[u], 16 if first else (I - u) * 8 + 16)
                    if not (first and u == 0):
                        act.wait_ge(mask_seen, I)
                    nc.scalar.square(square[:], mask[:, u]).then_inc(squared, 1)
                elif i == 6:
                    act.wait_ge(squared, I + 1)
                    nc.scalar.activation(sign[:], square[:], ACT.Sign, accum_out=nonzero[:, bass.ds(I, 1)]
                                         ).then_inc(mask_seen, 1)

            def sum_counts(n, fresh):
                act.wait_ge(counted, n + 1)
                if not fresh:
                    act.wait_ge(summed, n)
                nc.scalar.activation(counts[:], ps_c[0:TILES, :], ACT.Copy, accum_out=lows[:, bass.ds(n, 1)]
                                     ).then_inc(summed, 1)

            def iteration(I, u, first):
                for i in range(TILES):
                    step(I, i, u, first and u == 0)
                    if i == LAG - 1 and not (first and u == 0):
                        sum_counts(I - 1, first)
                    count_mask(I, u, i, first)

            over(act, pl.ITER, 2, iteration)
            for i in range(TILES, TILES + LAG + 5):
                step(pl.ITER - 1, i, 1, False)
            sum_counts(pl.ITER - 1, False)

        @block.vector
        def _(dve):
            STEPS = 2 * pl.ROUNDS

            def chunks(i, u, n0, n1):
                c = cand[:, u, i, :]
                for n in range(n0, n1):
                    ins = nc.vector.max(c[:, 8 + n:8 + n + 7 * CH + 1:CH], sc[:, i % 4, pl.cut[n]:pl.cut[n + 1]])
                if n1 == CH:
                    ins.then_inc(own, 1)

            def rounds(i, u, p, before):
                c, w, m = cand[:, u, i, :], work[:, i % 2, :], top[:, u, i, :]
                dve.wait_ge(own, before + p)
                if p == 0:
                    ins = nc.vector.max(c[:, 0:8], c[:, 8 + NA:NC])
                elif p == 1:
                    ins = nc.vector.max(m[:, 0:8], c[:, 0:8 + NA])
                elif p % 2 == 0:
                    r = p // 2
                    ins = nc.vector.match_replace(w, m[:, 8 * r - 8:8 * r], c[:, 0:8 + NA] if r == 1 else w, TAKEN)
                else:
                    r = p // 2
                    ins = nc.vector.max(m[:, 8 * r:8 * r + 8], w)
                ins.then_inc(thresh if p == STEPS - 1 else own, 1)

            def invert(Gn, gi, start):
                dve.wait_ge(out_turned, Gn + 1)
                if not (start and gi < 2):
                    dve.wait_ge(normed, Gn - 1)
                nc.vector.reciprocal(rden[:, gi % 2, :],
                                     ps_ou[:, P:2 * P].rearrange("p (j c) -> p j c", j=HG)[:, :, DK]).then_inc(recip, 1)

            def step(I, i, u, start):
                before = STEPS * i - (STEPS - 1 if start else 0)
                if i < TILES:
                    dve.wait_ge(copied[u], i + 1)
                if i == TILES // 2 and not start:
                    nc.vector.sem_clear(copied[1 - u])
                for p in range(STEPS):
                    if i < TILES:
                        chunks(i, u, CH * p // STEPS, CH * (p + 1) // STEPS)
                    if i <= TILES and not (start and i == 0):
                        rounds((i - 1) % TILES, u if i >= 1 else 1 - u, p, before)
                d = (i - LAG - 6) // HG
                if (i - LAG - 6) % HG == 0 and d < GI and not (start and d < 0):
                    invert(I * GI + d, d % GI, start)

            def iteration(I, u, first):
                if not (first and u == 0):
                    dve.wait_ge(own, STEPS * TILES - (STEPS - 1 if first else 0))
                    nc.vector.sem_clear(own)
                for i in range(TILES):
                    step(I, i, u, first and u == 0)

            over(dve, pl.ITER, 2, iteration)
            for i in range(TILES, TILES + LAG + 5):
                step(pl.ITER - 1, i, 1, False)

        @block.gpsimd
        def _(pool):
            nc.gpsimd.memset(ident[:], 0.0).then_inc(id0, 1)
            nc.gpsimd.memset(row_of[:], 0.0).then_inc(id0, 1)
            nc.gpsimd.memset(zeros[:], 0.0).then_inc(id0, 1)
            pool.wait_ge(id0, 3)
            nc.gpsimd.affine_select(out=ident[:], in_=ident[:], compare_op=ALU.not_equal, fill=1.0, base=0,
                                    pattern=[[-1, P]], channel_multiplier=1).then_inc(ident_ready, 1)
            pool.wait_ge(ident_ready, 1)
            nc.gpsimd.tensor_scalar(lowest[:], ident[:], -1.0e30, None, ALU.mult).then_inc(ident_ready, 1)
            for i in range(TILES):
                nc.gpsimd.memset(row_of[:, i, i:i + 1], 1.0).then_inc(ident_ready, 1)

            def mark_low(T, i, u, start):
                pool.wait_ge(thresh, T + 1)
                if not (start and i < 2):
                    pool.wait_ge(masked, T - 1)
                nc.gpsimd.tensor_tensor(nmax[:, u, i:i + 1], zeros[:, 0:1], top[:, u, i, 0:1], ALU.subtract)
                nc.gpsimd.tensor_scalar(low[:, i % 2, :], sc[:, i % 4, :], top[:, u, i, pl.TOPK - 1:pl.TOPK], None,
                                        ALU.is_lt).then_inc(lowed, 1)

            def iteration(I, u, first):
                for i in range(TILES):
                    mark_low(I * TILES + i, i, u, first and u == 0)

            over(pool, pl.ITER, 2, iteration)


def repair(nc, pl, io, scr, keep):
    G, TILES, KB, HG, DK, VW, KR, S2, QT = pl.G, pl.TILES, pl.KB, pl.HG, pl.DK, pl.VW, pl.KR, pl.S2, pl.QT
    NT = pl.ITER * TILES
    attn, lows, nonzero = keep["attn"], keep["lows"], keep["nonzero"]
    with ExitStack() as ctx:
        sb = lambda name, shape, dt=F32: ctx.enter_context(nc.sbuf_tensor(name, shape, dt))
        psum = lambda name, cols=512: ctx.enter_context(nc.psum_tensor(name, [P, cols], F32))
        sem = lambda name: ctx.enter_context(nc.semaphore(name))

        ones = sb("g_ones", [P, 1])
        ident = sb("g_ident", [P, P])
        countdown = sb("g_countdown", [1, NT])
        flat = sb("g_flat", [1, TILES, pl.ITER])
        bad = sb("g_bad", [1, NT])
        mask_bad = sb("g_mask_bad", [1, pl.TT])
        number = sb("g_number", [1, 1])
        eight = sb("g_eight", [1, 8])
        total = sb("g_total", [1, 1], I32)
        flagged_tiles = sb("g_flagged", [1, NT], I32)
        q = sb("g_q", [KR, P], BF16)
        k = sb("g_k", [KR, S2], BF16)
        v = sb("g_v", [P, KB, VW])
        mask = sb("g_mask", [P, S2], I32)
        s = sb("g_s", [P, S2])
        work = sb("g_work", [P, S2])
        top = sb("g_top", [P, pl.TOPK])
        nmax = sb("g_nmax", [P, 1])
        ex = sb("g_ex", [P, S2])
        exT = sb("g_exT", [P, S2])
        outT = sb("g_outT", [VW, P])
        rden = sb("g_rden", [P, 1])
        ps_s = psum("g_ps_s", S2)
        ps_t = [psum(f"g_ps_t{i}") for i in range(2)]
        ps_o = psum("g_ps_o", P)
        ps_u = psum("g_ps_u", VW)

        made = sem("g_made")
        own = sem("g_own")
        cleared = sem("g_cleared")
        again = sem("g_again")
        sums_ready = sem("g_sums_ready")
        flags_ready = sem("g_flags_ready")
        free = sem("g_free")
        v_free = sem("g_v_free")
        in_v = sem("g_in_v")
        in_flat = sem("g_in_flat")
        in_pe = sem("g_in_pe")
        in_dve = sem("g_in_dve")
        scored = sem("g_scored")
        topped = sem("g_topped")
        expd = sem("g_expd")
        probs = sem("g_probs")
        turned = sem("g_turned")
        turned_sb = sem("g_turned_sb")
        out_ready = sem("g_out_ready")
        out_sb = sem("g_out_sb")
        out_turned = sem("g_out_turned")
        block = ctx.enter_context(nc.Block())

        def flagged(eng, body):
            eng.wait_ge(flags_ready, 1)
            n = eng.value_load(total[0:1, 0:1], min_val=0, max_val=NT)
            with eng.If(n > 0):
                with eng.Fori(0, n) as i:
                    tile = eng.value_load(flagged_tiles[0:1, bass.ds(i, 1)], min_val=0, max_val=NT - 1)
                    body(tile // TILES, tile % TILES // HG, tile % HG)

        def take(eng, signal, n=1):
            eng.wait_ge(signal, n)
            eng.sem_clear(signal)

        @block.gpsimd
        def _(pool):
            nc.gpsimd.memset(ident[:], 0.0).then_inc(made, 1)
            nc.gpsimd.memset(ones[:], 1.0).then_inc(made, 1)
            pool.wait_ge(made, 2)
            nc.gpsimd.affine_select(out=ident[:], in_=ident[:], compare_op=ALU.not_equal, fill=1.0, base=0,
                                    pattern=[[-1, P]], channel_multiplier=1).then_inc(made, 1)
            nc.gpsimd.iota(countdown[:], pattern=[[-1, NT]], base=NT, channel_multiplier=0,
                           allow_small_or_imprecise_dtypes=True).then_inc(made, 1)

            def tile(I, t, j):
                take(pool, again)
                nc.gpsimd.memset(s[:], NEG).then_inc(cleared, 1)

            flagged(pool, tile)

        @block.sync
        def _(sp):
            sp.dma_start(flat[:], lows[:]).then_inc(in_flat, 16)

            def tile(I, t, j):
                take(sp, free)
                for term, part, n in pl.q_spans:
                    sp.dma_start(q[term * DK:(term + n) * DK, :],
                                 scr["q"].rearrange("i (r j) n -> i r j n", j=HG)[I, part * DK:(part + n) * DK, j, bass.ds(t * P, P)]
                                 ).then_inc(in_pe, 16)
                for term, part, n in pl.k_spans:
                    sp.dma_start(k[term * DK:(term + n) * DK, :],
                                 scr["k"].rearrange("i (r j) n -> i r j n", j=HG)[I, part * DK:(part + n) * DK, j, :]
                                 ).then_inc(in_pe, 16)
                sp.dma_start(mask[:], io["mask"].rearrange("b (t p) s -> (b t) p s", p=P)[(I // G) * QT + t]
                             ).then_inc(in_dve, 16)
                take(sp, v_free)
                sp.dma_start(v[:], scr["v"].rearrange("i p (k h c) -> i p k h c", k=KB, h=HG)[I, :, :, j, :]
                             ).then_inc(in_v, 16)

            flagged(sp, tile)

        @block.tensor
        def _(pe):
            pe.wait_ge(made, 3)
            nc.tensor.matmul(ps_t[1][0:1, 0:pl.TT], ones[:], nonzero[:], start=True, stop=True).then_inc(sums_ready, 1)

            def tile(I, t, j):
                take(pe, in_pe, 16 * (len(pl.q_spans) + len(pl.k_spans)))
                for h in range(S2 // 512):
                    mm = nc.tensor.matmul(ps_s[:, h * 512:(h + 1) * 512], q[:], k[:, h * 512:(h + 1) * 512],
                                          start=True, stop=True)
                mm.then_inc(scored, 1)
                take(pe, probs)
                for c in range(KB):
                    mm = nc.tensor.transpose(ps_t[c // 4][:, c % 4 * P:(c % 4 + 1) * P], ex[:, c * P:(c + 1) * P], ident[:])
                mm.then_inc(turned, 1)
                take(pe, turned_sb, 2)
                take(pe, in_v, 16)
                for c in range(KB):
                    mm = nc.tensor.matmul(ps_o[0:VW, :], v[:, c, :], exT[:, c * P:(c + 1) * P],
                                          start=(c == 0), stop=(c == KB - 1))
                mm.then_inc(out_ready, 1)
                take(pe, out_sb)
                nc.tensor.transpose(ps_u[:, 0:VW], outT[:], ident[0:VW, 0:VW]).then_inc(out_turned, 1)

            flagged(pe, tile)

        @block.scalar
        def _(act):
            def tile(I, t, j):
                take(act, topped)
                nc.scalar.activation(ex[:], s[:], ACT.Exp, bias=nmax[:]).then_inc(expd, 1)
                take(act, turned)
                for h in range(2):
                    nc.scalar.copy(exT[:, h * 512:(h + 1) * 512], ps_t[h][:]).then_inc(turned_sb, 1)

            flagged(act, tile)

        @block.vector
        def _(dve):
            V = nc.vector
            count = [0]

            def link(ins):
                count[0] += 1
                ins.then_inc(own, 1)
                dve.wait_ge(own, count[0])

            dve.wait_ge(sums_ready, 1)
            link(V.tensor_scalar(mask_bad[:], ps_t[1][0:1, 0:pl.TT], float(P * S2), None, ALU.not_equal))
            dve.wait_ge(in_flat, 16)
            link(V.tensor_scalar(bad[:].rearrange("p (i n) -> p n i", n=TILES), flat[:], float(P * (S2 - pl.TOPK)), None,
                                 ALU.not_equal))
            by_mask = mask_bad[:].rearrange("p (b t) -> p b t", t=QT).unsqueeze(3).broadcast_to([1, pl.B, QT, HG])
            for g in range(G):
                part = bad[:].rearrange("p (b g t j) -> p b g t j", g=G, t=QT, j=HG)[:, :, g]
                ins = V.tensor_tensor(part, part, by_mask, ALU.max)
            link(ins)
            link(V.tensor_reduce(number[:], bad[:], AX_X, ALU.add))
            link(V.tensor_copy(total[:], number[:]))
            dve.wait_ge(made, 4)
            link(V.tensor_tensor(bad[:], bad[:], countdown[:], ALU.mult))
            n = dve.value_load(total[0:1, 0:1], min_val=0, max_val=NT)
            with dve.If(n > 0):
                with dve.Fori(0, (n + 7) // 8) as i:
                    dve.sem_clear(own)
                    count[0] = 0
                    link(V.max(eight[:], bad[:]))
                    link(V.match_replace(bad[:], eight[:], bad[:], -1.0))
                    link(V.tensor_scalar(flagged_tiles[:, bass.ds(i * 8, 8)], eight[:], -1.0, float(NT), ALU.mult, ALU.add))
            dve.sem_inc(free, 1)
            dve.sem_inc(v_free, 1)
            dve.sem_inc(again, 1)
            dve.sem_clear(own)
            dve.sem_inc(flags_ready, 1)

            def tile(I, t, j):
                count[0] = 0
                take(dve, in_dve, 16)
                take(dve, cleared)
                take(dve, scored)
                link(V.copy_predicated(s[:], mask[:], ps_s[:]))
                dve.sem_inc(free, 1)
                link(V.max(top[:, 0:8], s[:]))
                V.tensor_scalar(nmax[:], top[:, 0:1], -1.0, None, ALU.mult).then_inc(topped, 1)
                for r in range(pl.ROUNDS):
                    if r:
                        link(V.max(top[:, 8 * r:8 * r + 8], work[:]))
                    link(V.match_replace(work[:], top[:, 8 * r:8 * r + 8], work[:] if r else s[:], TAKEN))
                take(dve, expd)
                dve.sem_inc(again, 1)
                V.scalar_tensor_tensor(out=ex[:], in0=work[:], scalar=TAKEN / 2, in1=ex[:], op0=ALU.is_lt, op1=ALU.mult
                                       ).then_inc(probs, 1)
                take(dve, out_ready)
                V.tensor_copy(outT[:], ps_o[0:VW, :]).then_inc(out_sb, 1)
                take(dve, out_turned)
                link(V.reciprocal(rden[:], ps_u[:, DK:DK + 1]))
                link(V.tensor_scalar(attn[:, I * QT + t, bass.ds(j * DK, DK)], ps_u[:, 0:DK], rden[:], None, ALU.mult))
                dve.sem_clear(own)
                dve.sem_inc(v_free, 1)

            flagged(dve, tile)


def route(nc, pl, io, scr, keep):
    B, QT, TT, D, E, KD = pl.B, pl.QT, pl.TT, pl.D, pl.E, pl.KD
    GD = pl.HG * pl.DK
    CAP, K2 = pl.CAP, 2
    ROWS = E * K2 * CAP
    attn, x1, slot_to, slot_from, weight = (keep[n] for n in ("attn", "x1", "slot_to", "slot_from", "weight"))
    with ExitStack() as ctx:
        sb = lambda name, shape, dt=F32: ctx.enter_context(nc.sbuf_tensor(name, shape, dt))
        psum = lambda name, cols=512: ctx.enter_context(nc.psum_tensor(name, [P, cols], F32))
        sem = lambda name: ctx.enter_context(nc.semaphore(name))

        xn = sb("r_xn", [P, TT, D])
        wo = sb("r_wo", [P, KD, D])
        gate = sb("r_gate", [P, KD, E])
        bo = sb("r_bo", [P, D])
        g = sb("r_g", [P, 2])
        tg = sb("r_tg", [P, 2])
        ident = sb("r_ident", [P, P])
        upto = sb("r_upto", [P, P])
        ones = sb("r_ones", [P, P])
        lane = sb("r_lane", [P, E])
        xin = sb("r_xin", [P, 2, QT, D])
        ain = sb("r_ain", [P, 2, QT, D])
        xs = sb("r_xs", [P, 2, QT, D])
        aT = sb("r_aT", [P, QT, D])
        xT = sb("r_xT", [P, QT, D])
        stats = sb("r_stats", [P, 2, QT, 6])
        mv = sb("r_mv", [P, 2, QT, 2])
        veps = sb("r_veps", [P, 2, QT])
        std = sb("r_std", [P, 2, QT])
        rstd = sb("r_rstd", [P, 2, QT])
        aO = sb("r_aO", [P, D])
        order = sb("r_order", [P, 2, QT, 8])
        index = sb("r_index", [P, 2, QT, 8], U32)
        logit = sb("r_logit", [P, 2, QT, E])
        best = sb("r_best", [P, TT, 8])
        which = sb("r_which", [P, TT, 8], U32)
        chosen = sb("r_chosen", [P, TT, K2])
        onehot = sb("r_onehot", [P, TT, K2, E])
        before = [sb(f"r_before{i}", [P, TT, K2, E]) for i in range(2)]
        place = sb("r_place", [P, TT, K2, E])
        at = sb("r_at", [P, TT, K2])
        valid = sb("r_valid", [P, TT, K2])
        first = sb("r_first", [P, TT, K2])
        tmp = sb("r_tmp", [P, TT, K2])
        e2 = sb("r_e2", [P, TT])
        w1 = sb("r_w1", [P, TT])
        ps_a = [psum(f"r_ps_a{i}") for i in range(2)]
        ps_w = [psum(f"r_ps_w{i}") for i in range(2)]
        ps_x = [psum(f"r_ps_x{i}") for i in range(2)]
        ps_l = psum("r_ps_l")
        ps_n = psum("r_ps_n")

        w_in = sem("r_w_in")
        made = sem("r_made")
        a_in = sem("r_a_in")
        xn_kept = sem("r_xn_kept")
        x_in = [sem(f"r_x_in{u}") for u in range(2)]
        a_turned = sem("r_a_turned")
        a_sb = sem("r_a_sb")
        o_full = sem("r_o_full")
        x1_done = sem("r_x1_done")
        x1_kept = sem("r_x1_kept")
        var_done = sem("r_var_done")
        std_done = sem("r_std_done")
        xn_done = sem("r_xn_done")
        x_turned = sem("r_x_turned")
        x_sb = sem("r_x_sb")
        l_full = sem("r_l_full")
        l_sb = sem("r_l_sb")
        tanh_done = sem("r_tanh_done")
        own = sem("r_own")
        hot = sem("r_hot")
        counted = sem("r_counted")
        e_in = sem("r_e_in")
        e_out = sem("r_e_out")
        slots_done = sem("r_slots_done")
        weights_done = sem("r_weights_done")
        sent = sem("r_sent")
        block = ctx.enter_context(nc.Block())

        @block.sync
        def _(sp):
            sp.dma_start(wo[:], io["woT"].rearrange("(k p) n -> p k n", p=P)).then_inc(w_in, 16)
            sp.dma_start(gate[:], io["gateT"].rearrange("(k p) n -> p k n", p=P)).then_inc(w_in, 16)
            sp.dma_start(bo[:], io["bo"].partition_broadcast(P)).then_inc(w_in, 16)
            for i, name in enumerate(("g_xattn", "g_ffn")):
                sp.dma_start(g[:, i:i + 1], io[name][0].partition_broadcast(P)).then_inc(w_in, 16)

            def load(b, u, start):
                if not start:
                    sp.wait_ge(x1_done, QT * (b - 1))
                    keep_x1(b - 2)
                sp.dma_start(xin[:, u], io["x"][b].rearrange("(t p) d -> p t d", p=P)).then_inc(x_in[u], 16)

            def keep_x1(b):
                sp.dma_start(scr["x1"][b], x1[:, bass.ds(b * QT, QT), :]).then_inc(x1_kept, 16)

            over(sp, B, 2, load)
            for b in (B - 2, B - 1):
                sp.wait_ge(x1_done, QT * (b + 1))
                keep_x1(b)
            sp.wait_ge(x1_kept, 16 * B)

        @block.gpsimd
        def _(pool):
            nc.gpsimd.memset(ident[:], 0.0).then_inc(made, 1)
            nc.gpsimd.memset(ones[:], 1.0).then_inc(made, 1)
            nc.gpsimd.iota(lane[:], pattern=[[1, E]], base=0, channel_multiplier=0,
                           allow_small_or_imprecise_dtypes=True).then_inc(made, 1)
            pool.wait_ge(made, 3)
            nc.gpsimd.affine_select(out=ident[:], in_=ident[:], compare_op=ALU.not_equal, fill=1.0, base=0,
                                    pattern=[[-1, P]], channel_multiplier=1).then_inc(made, 1)
            nc.gpsimd.affine_select(out=upto[:], in_=ones[:], compare_op=ALU.is_ge, fill=0.0, base=0,
                                    pattern=[[1, P]], channel_multiplier=-1).then_inc(made, 1)

            def gather(b, u, start):
                if not start:
                    pool.wait_ge(a_turned, 2 * (b - 1))
                for k in range(pl.G):
                    ins = nc.gpsimd.tensor_copy(ain[:, u, :, k * GD:(k + 1) * GD],
                                                attn[:, bass.ds(b * (pl.G * QT) + k * QT, QT), :])
                ins.then_inc(a_in, 1)

            def keep_rows(b, u):
                pool.wait_ge(xn_done, b + 1)
                nc.gpsimd.tensor_copy(xn[:, bass.ds(b * QT, QT), :], xs[:, u]).then_inc(xn_kept, 1)

            def step(b, u, start):
                gather(b, u, start)
                if not (start and b == 0):
                    keep_rows(b - 1, 1 - u)

            over(pool, B, 2, step)
            keep_rows(B - 1, 1)
            pool.wait_ge(xn_kept, B)
            pool.wait_ge(slots_done, 2)
            for n in range(TT):
                for k in range(K2):
                    pool.indirect_dma_start(
                        out=scr["disp"], out_offset=bass.IndirectOffsetOnAxis(ap=slot_to[:, n, k:k + 1], axis=0),
                        in_=xn[:, n, :], in_offset=None, bounds_check=ROWS - 1, oob_is_err=False).then_inc(sent, 16)
            pool.wait_ge(sent, 16 * TT * K2)

        @block.tensor
        def _(pe):
            pe.wait_ge(w_in, 16 * 5)
            pe.wait_ge(made, 5)

            def outputs(b, u, start):
                for t in range(QT):
                    i = t % 2
                    if t == 0:
                        pe.wait_ge(a_in, b + 1)
                    if i == 0 and not (start and b == 0):
                        pe.wait_ge(a_sb, 2 * b + t // 2 - 1)
                    for k in range(KD):
                        mm = nc.tensor.transpose(ps_a[t // 2][:, i * D + k * P:i * D + (k + 1) * P],
                                                 ain[:, u, t, k * P:(k + 1) * P], ident[:])
                    if i == 1:
                        mm.then_inc(a_turned, 1)
                for t in range(QT):
                    i = t % 2
                    if i == 0:
                        pe.wait_ge(a_sb, 2 * b + t // 2 + 1)
                        if not (start and b == 0):
                            pe.wait_ge(x1_done, QT * (b - 1) + t + 2)
                    for k in range(KD):
                        mm = nc.tensor.matmul(ps_w[t // 2][:, i * D:(i + 1) * D], aT[:, t, k * P:(k + 1) * P], wo[:, k, :],
                                              start=(k == 0), stop=(k == KD - 1))
                    if i == 1:
                        mm.then_inc(o_full, 1)

            def logits(b, u, start):
                for t in range(QT):
                    i = t % 2
                    if i == 0:
                        pe.wait_ge(xn_done, b + 1)
                        if not start:
                            pe.wait_ge(x_sb, 2 * b + t // 2 - 1)
                    for k in range(KD):
                        mm = nc.tensor.transpose(ps_x[t // 2][:, i * D + k * P:i * D + (k + 1) * P],
                                                 xs[:, u, t, k * P:(k + 1) * P], ident[:])
                    if i == 1:
                        mm.then_inc(x_turned, 1)
                if not start:
                    pe.wait_ge(l_sb, b)
                for t in range(QT):
                    pe.wait_ge(x_sb, 2 * b + t // 2 + 1)
                    for k in range(KD):
                        mm = nc.tensor.matmul(ps_l[:, t * E:(t + 1) * E], xT[:, t, k * P:(k + 1) * P], gate[:, k, :],
                                              start=(k == 0), stop=(k == KD - 1))
                mm.then_inc(l_full, 1)

            def step(b, u, start):
                outputs(b, u, start)
                if not (start and b == 0):
                    logits(b - 1, 1 - u, start and b == 1)

            over(pe, B, 2, step)
            logits(B - 1, 1, False)
            pe.wait_ge(hot, 1)
            nc.tensor.matmul(ps_n[:, 0:TT * K2 * E], upto[:], onehot[:].rearrange("p t k e -> p (t k e)"),
                             start=True, stop=True)
            nc.tensor.matmul(ps_l[:, 0:TT * K2 * E], ones[:], onehot[:].rearrange("p t k e -> p (t k e)"),
                             start=True, stop=True).then_inc(counted, 1)

        @block.scalar
        def _(act):
            act.wait_ge(w_in, 16 * 5)
            nc.scalar.activation(tg[:], g[:], ACT.Tanh).then_inc(tanh_done, 1)

            def copies(b, u, start):
                for h in range(2):
                    act.wait_ge(a_turned, 2 * b + h + 1)
                    if not (start and b == 0):
                        act.wait_ge(o_full, 2 * b)
                    nc.scalar.copy(aT[:, 2 * h:2 * h + 2, :].rearrange("p t d -> p (t d)"), ps_a[h][:]).then_inc(a_sb, 1)

            def turned(b, u, start):
                for h in range(2):
                    act.wait_ge(x_turned, 2 * b + h + 1)
                    if not start:
                        act.wait_ge(l_full, b)
                    nc.scalar.copy(xT[:, 2 * h:2 * h + 2, :].rearrange("p t d -> p (t d)"), ps_x[h][:]).then_inc(x_sb, 1)

            def step(b, u, start):
                copies(b, u, start)
                if not (start and b == 0):
                    turned(b - 1, 1 - u, start and b == 1)
                act.wait_ge(var_done, b + 1)
                nc.scalar.activation(std[:, u], veps[:, u], ACT.Sqrt).then_inc(std_done, 1)

            over(act, B, 2, step)
            turned(B - 1, 1, False)
            act.wait_ge(e_in, 1)
            nc.scalar.activation(e2[:], tmp[:, :, 0], ACT.Exp).then_inc(e_out, 1)

        @block.vector
        def _(dve):
            count = [0]

            def link(ins):
                count[0] += 1
                ins.then_inc(own, 1)
                dve.wait_ge(own, count[0])

            def residual(b, u, start):
                for t in range(QT):
                    if t % 2 == 0:
                        dve.wait_ge(o_full, 2 * b + t // 2 + 1)
                    link(nc.vector.tensor_tensor(aO[:], ps_w[t // 2][:, t % 2 * D:(t % 2 + 1) * D], bo[:], ALU.add))
                    link(nc.vector.scalar_tensor_tensor(out=x1[:, b * QT + t, :], in0=aO[:], scalar=tg[:, 0:1],
                                                        in1=xin[:, u, t, :], op0=ALU.mult, op1=ALU.add))
                for t in range(QT):
                    ins = nc.vector.bn_stats(stats[:, u, t, :], x1[:, b * QT + t, :])
                link(ins)
                nc.vector.bn_aggr(mv[:, u, 0, :], stats[:, u, 0, :]).then_inc(x1_done, QT)
                for t in range(1, QT):
                    ins = nc.vector.bn_aggr(mv[:, u, t, :], stats[:, u, t, :])
                link(ins)
                nc.vector.tensor_scalar(veps[:, u], mv[:, u, :, 1], LN_EPS, None, ALU.add).then_inc(var_done, 1)

            def choose(b, u, start):
                dve.wait_ge(l_full, b + 1)
                link(nc.vector.tensor_copy(logit[:, u], ps_l[:, 0:QT * E].rearrange("p (t e) -> p t e", e=E)))
                nc.vector.max(order[:, u, 0, :], logit[:, u, 0, :]).then_inc(l_sb, 1)
                for t in range(1, QT):
                    ins = nc.vector.max(order[:, u, t, :], logit[:, u, t, :])
                link(ins)
                for t in range(QT):
                    ins = nc.vector.max_index(index[:, u, t, :], order[:, u, t, :], logit[:, u, t, :])
                link(ins)
                nc.vector.tensor_copy(best[:, bass.ds(b * QT, QT), :], order[:, u])
                link(nc.vector.tensor_copy(which[:, bass.ds(b * QT, QT), :], index[:, u]))

            def norm(b, u, start):
                dve.wait_ge(std_done, b + 1)
                link(nc.vector.reciprocal(rstd[:, u], std[:, u]))
                if not start:
                    dve.wait_ge(xn_kept, b - 1)
                for t in range(QT):
                    ins = nc.vector.tensor_scalar(xs[:, u, t, :], x1[:, b * QT + t, :], mv[:, u, t, 0:1],
                                                  rstd[:, u, t:t + 1], ALU.subtract, ALU.mult)
                ins.then_inc(xn_done, 1)

            def step(b, u, start):
                if not (start and b == 0):
                    dve.wait_ge(own, count[0])
                    nc.vector.sem_clear(own)
                count[0] = 0
                dve.wait_ge(x_in[u], 16 if start else (b - u) * 8 + 16)
                residual(b, u, start)
                if not (start and b == 0):
                    choose(b - 1, 1 - u, start and b == 1)
                norm(b, u, start)

            dve.wait_ge(w_in, 16 * 5)
            dve.wait_ge(tanh_done, 1)
            dve.wait_ge(made, 3)
            over(dve, B, 2, step)
            nc.vector.sem_clear(own)
            count[0] = 0
            choose(B - 1, 1, False)

            V = nc.vector
            link(V.tensor_copy(chosen[:], which[:, :, 0:K2]))
            for k in range(K2):
                ins = V.tensor_tensor(onehot[:, :, k, :], lane[:].unsqueeze(1).broadcast_to([P, TT, E]),
                                      chosen[:, :, k:k + 1].broadcast_to([P, TT, E]), ALU.is_equal)
            ins.then_inc(hot, 1)
            link(V.tensor_tensor(tmp[:, :, 0], best[:, :, 1], best[:, :, 0], ALU.subtract))
            V.memset(before[0][:, 0:1], 0.0).then_inc(e_in, 1)
            link(V.tensor_scalar(first[:], chosen[:], float(K2 * CAP), None, ALU.mult))
            link(V.tensor_scalar(first[:, :, 1], first[:, :, 1], float(CAP), None, ALU.add))
            dve.wait_ge(counted, 1)
            flat = lambda ap: ap.rearrange("p t k e -> p t (k e)")
            tiles = lambda ps: ps[:, 0:TT * K2 * E].rearrange("p (t c) -> p t c", t=TT)
            link(V.tensor_copy(flat(before[0][:, 1:TT]), tiles(ps_l)[:, 0:TT - 1, :]))
            s, a = 1, 0
            while s < TT:
                V.tensor_copy(flat(before[1 - a][:, 0:s]), flat(before[a][:, 0:s]))
                link(V.tensor_tensor(flat(before[1 - a][:, s:TT]), flat(before[a][:, s:TT]), flat(before[a][:, 0:TT - s]), ALU.add))
                s, a = 2 * s, 1 - a
            link(V.tensor_tensor(flat(place[:]), flat(before[a][:]), tiles(ps_n), ALU.add))
            link(V.tensor_tensor(flat(place[:]), flat(place[:]), flat(onehot[:]), ALU.mult))
            link(V.tensor_reduce(at[:], place[:], AX_X, ALU.add))
            link(V.tensor_scalar(valid[:], at[:], float(CAP), None, ALU.is_le))
            dve.wait_ge(e_out, 1)
            link(V.scalar_tensor_tensor(out=tmp[:], in0=at[:], scalar=-1.0, in1=valid[:], op0=ALU.add, op1=ALU.mult))
            link(V.tensor_tensor(first[:], first[:], tmp[:], ALU.add))
            V.tensor_copy(slot_from[:], first[:]).then_inc(slots_done, 1)
            link(V.tensor_scalar(tmp[:], valid[:], -float(1 << 20), float(1 << 20), ALU.mult, ALU.add))
            link(V.tensor_tensor(tmp[:], tmp[:], first[:], ALU.add))
            V.tensor_copy(slot_to[:], tmp[:]).then_inc(slots_done, 1)
            link(V.tensor_scalar(w1[:], e2[:], 1.0, None, ALU.add))
            link(V.reciprocal(w1[:], w1[:]))
            V.tensor_copy(weight[:, :, 0], w1[:])
            link(V.tensor_tensor(weight[:, :, 1], w1[:], e2[:], ALU.mult))
            V.scalar_tensor_tensor(out=weight[:], in0=weight[:], scalar=tg[:, 1:2], in1=valid[:], op0=ALU.mult,
                                   op1=ALU.mult).then_inc(weights_done, 1)
            dve.wait_ge(weights_done, 1)


def experts(nc, pl, io, scr):
    D, E, F, KD, CAP = pl.D, pl.E, pl.F, pl.KD, pl.CAP
    FB = F // P
    RT = 2 if (2 * CAP) % (2 * P) == 0 else 1
    R = RT * P
    NCH = 2 * CAP // R
    with ExitStack() as ctx:
        sb = lambda name, shape, dt=F32: ctx.enter_context(nc.sbuf_tensor(name, shape, dt))
        psum = lambda name, cols=512: ctx.enter_context(nc.psum_tensor(name, [P, cols], F32))
        sem = lambda name: ctx.enter_context(nc.semaphore(name))

        ident = sb("e_ident", [P, P])
        raw = sb("e_raw", [P, 2, KD * F])
        wh, wl = (sb(n, [P, 2, 3, KD * F], F32R) for n in ("e_wh", "e_wl"))
        assert KD * F == FB * D
        xin = sb("e_xin", [P, 2, RT, D])
        xh, xl = (sb(n, [P, 2, KD, R], F32R) for n in ("e_xh", "e_xl"))
        th = sb("e_th", [P, 2, R])
        sg = sb("e_sg", [P, 2, R])
        h = sb("e_h", [P, 2, R])
        hh, hl = (sb(n, [P, 2, FB, R], F32R) for n in ("e_hh", "e_hl"))
        y = sb("e_y", [P, 2, RT, D])
        ps_x = psum("e_ps_x")
        ps_gu = [psum(f"e_ps_gu{i}") for i in range(4)]
        ps_y = [psum(f"e_ps_y{i}") for i in range(2)]

        id0 = sem("e_id0")
        ident_ready = sem("e_ident_ready")
        raw_in = [sem(f"e_raw_in{u}") for u in range(2)]
        x_in = [sem(f"e_x_in{u}") for u in range(2)]
        x_turned = sem("e_x_turned")
        x_high = sem("e_x_high")
        x_cut = sem("e_x_cut")
        w_high = sem("e_w_high")
        w_cut = sem("e_w_cut")
        gu_full = sem("e_gu_full")
        th_done = sem("e_th_done")
        sg_done = sem("e_sg_done")
        h_done = sem("e_h_done")
        h_high = sem("e_h_high")
        h_cut = sem("e_h_cut")
        y_full = sem("e_y_full")
        y_sb = sem("e_y_sb")
        stored = [sem(f"e_stored{u}") for u in range(2)]
        block = ctx.enter_context(nc.Block())

        @block.gpsimd
        def _(pool):
            nc.gpsimd.memset(ident[:], 0.0).then_inc(id0, 1)
            pool.wait_ge(id0, 1)
            nc.gpsimd.affine_select(out=ident[:], in_=ident[:], compare_op=ALU.not_equal, fill=1.0, base=0,
                                    pattern=[[-1, P]], channel_multiplier=1).then_inc(ident_ready, 1)

            def cut_weights(e, u, start):
                for n in range(3):
                    pool.wait_ge(w_high, 3 * e + n + 1)
                    nc.gpsimd.tensor_tensor(wl[:, u, n], raw[:, (u + n) % 2], wh[:, u, n].bitcast(F32), ALU.subtract
                                            ).then_inc(w_cut, 1)

            over(pool, E, 2, cut_weights)

        @block.sync
        def _(sp):
            def expert(e, u, start):
                for n, name in enumerate(("wgT", "wuT", "wdT")):
                    if not (start and 3 * u + n < 2):
                        sp.wait_ge(w_cut, 3 * e + n - 1)
                    sp.dma_start(raw[:, (u + n) % 2, :].rearrange("p (k f) -> p k f", k=FB if n == 2 else KD),
                                 io[name][e].rearrange("(k p) f -> p k f", p=P)).then_inc(raw_in[(u + n) % 2], 16)
                for c in range(NCH):
                    C, s = e * NCH + c, (u * NCH + c) % 2
                    if not (start and u * NCH + c < 2):
                        sp.wait_ge(x_turned, C - 1)
                    sp.dma_start(xin[:, s], scr["disp_c"][C].rearrange("(r p) d -> p r d", p=P)).then_inc(x_in[s], 16)

            over(sp, E, 2, expert)

        @block.tensor
        def _(pe):
            pe.wait_ge(ident_ready, 1)

            def turn(C, s, n, first):
                pe.wait_ge(x_in[s], n)
                if not first:
                    pe.wait_ge(x_cut, C)
                for k in range(KD):
                    for r in range(RT):
                        mm = nc.tensor.transpose(ps_x[:, k * R + r * P:k * R + (r + 1) * P],
                                                 xin[:, s, r, k * P:(k + 1) * P], ident[:])
                mm.then_inc(x_turned, 1)

            def product(out, parts_a, parts_b):
                n = len(parts_a)
                for k, ((ah, al), (bh, bl)) in enumerate(zip(parts_a, parts_b)):
                    nc.tensor.matmul(out, al, bh, start=(k == 0), stop=False)
                    nc.tensor.matmul(out, ah, bl, start=False, stop=False)
                    mm = nc.tensor.matmul(out, ah, bh, start=False, stop=(k == n - 1))
                return mm

            def up(C, s, u, start):
                pe.wait_ge(x_cut, C + 1)
                for f in range(FB):
                    n = C * FB + f
                    if not (start and f < 4):
                        pe.wait_ge(h_done, n - 3)
                    for i in range(2):
                        part = [slice(k * F + f * P, k * F + (f + 1) * P) for k in range(KD)]
                        mm = product(ps_gu[f % 4][:, i * R:(i + 1) * R],
                                     [(wh[:, u, i, c], wl[:, u, i, c]) for c in part],
                                     [(xh[:, s, k, :], xl[:, s, k, :]) for k in range(KD)])
                    mm.then_inc(gu_full, 1)

            def down(C, s, u, start):
                if not start:
                    pe.wait_ge(y_sb, C - 1)
                pe.wait_ge(h_cut, (C + 1) * FB)
                for r in range(RT):
                    rows = slice(r * P, (r + 1) * P)
                    mm = product(ps_y[s][:, r * D:(r + 1) * D],
                                 [(hh[:, s, f, rows], hl[:, s, f, rows]) for f in range(FB)],
                                 [(wh[:, u, 2, f * D:(f + 1) * D], wl[:, u, 2, f * D:(f + 1) * D]) for f in range(FB)])
                mm.then_inc(y_full, 1)

            def expert(e, u, start):
                pe.wait_ge(w_cut, 3 * e + 3)
                for c in range(NCH):
                    C, q = e * NCH + c, u * NCH + c
                    s = q % 2
                    turn(C, s, 16 * (q // 2 + 1) if start else (e - u) * (8 * NCH) + 16 * (q // 2 + 1), start and q == 0)
                    if not (start and q < 2):
                        down(C - 2, s, u if c >= 2 else 1 - u, start and q < 4)
                    up(C, s, u, start and q == 0)

            over(pe, E, 2, expert)
            for q in (2 * NCH - 2, 2 * NCH - 1):
                down((E - 2) * NCH + q, q % 2, 1, False)

        @block.scalar
        def _(act):
            def expert(e, u, start):
                for c in range(NCH):
                    C, q = e * NCH + c, u * NCH + c
                    s = q % 2
                    act.wait_ge(x_turned, C + 1)
                    if not (start and q < 2):
                        act.wait_ge(gu_full, FB * (C - 1))
                    nc.scalar.copy(xh[:, s].rearrange("p k r -> p (k r)"), ps_x[:, 0:KD * R]).then_inc(x_high, 1)
                    if not (start and q < 2):
                        store(C - 2, s, start and q < 4, q - 2, start, e, u)
                    for f in range(FB):
                        n = C * FB + f
                        act.wait_ge(gu_full, n + 1)
                        if not (start and q == 0 and f < 2):
                            act.wait_ge(sg_done, n - 1)
                        nc.scalar.activation(th[:, f % 2, :], ps_gu[f % 4][:, 0:R], ACT.Tanh, scale=0.5).then_inc(th_done, 1)

            def store(C, s, fresh, q, start, e, u):
                act.wait_ge(y_full, C + 1)
                if not fresh:
                    act.wait_ge(stored[s], 16 * (q // 2) if start else (e - u) * (8 * NCH) + 16 * (q // 2))
                nc.scalar.copy(y[:, s].rearrange("p r d -> p (r d)"), ps_y[s][:, 0:RT * D]).then_inc(y_sb, 1)
                act.wait_ge(y_sb, C + 1)
                act.dma_start(scr["eout_c"][C].rearrange("(r p) d -> p r d", p=P), y[:, s]).then_inc(stored[s], 16)

            over(act, E, 2, expert)
            for q in (2 * NCH - 2, 2 * NCH - 1):
                store((E - 2) * NCH + q, q % 2, False, q, False, E - 1, 1)
            for s in range(2):
                act.wait_ge(stored[s], 16 * ((E * NCH + 1 - s) // 2))

        @block.vector
        def _(dve):
            def cut_x(C, s):
                dve.wait_ge(x_high, C + 1)
                nc.vector.tensor_tensor(xl[:, s].rearrange("p k r -> p (k r)"), ps_x[:, 0:KD * R],
                                        xh[:, s].rearrange("p k r -> p (k r)").bitcast(F32), ALU.subtract).then_inc(x_cut, 1)

            def high(n, s, f):
                dve.wait_ge(h_done, n + 1)
                nc.vector.tensor_copy(hh[:, s, f, :], h[:, f % 2, :]).then_inc(h_high, 1)

            def lower(n, s, f):
                dve.wait_ge(h_high, n + 1)
                nc.vector.tensor_tensor(hl[:, s, f, :], h[:, f % 2, :], hh[:, s, f, :].bitcast(F32), ALU.subtract
                                        ).then_inc(h_cut, 1)

            def high_weight(e, u, n, start):
                dve.wait_ge(raw_in[(u + n) % 2], 16 * ((3 * u + n) // 2 + 1) + (0 if start else (e - u) * 24))
                if not start and n == 0:
                    dve.wait_ge(y_full, NCH * (e - 1))
                nc.vector.tensor_copy(wh[:, u, n], raw[:, (u + n) % 2]).then_inc(w_high, 1)

            def expert(e, u, start, last=False):
                for c in range(NCH):
                    C, q = e * NCH + c, u * NCH + c
                    s = q % 2
                    cut_x(C, s)
                    if c >= NCH - 3 and not last:
                        high_weight(e + 1, 1 - u, c - NCH + 3, start and u == 0)
                    for f in range(FB):
                        n = C * FB + f
                        dve.wait_ge(th_done, n + 1)
                        if not (start and q == 0 and f < 2):
                            dve.wait_ge(h_done, n - 1)
                        nc.vector.scalar_tensor_tensor(out=sg[:, f % 2, :], in0=th[:, f % 2, :], scalar=1.0,
                                                       in1=ps_gu[f % 4][:, 0:R], op0=ALU.add, op1=ALU.mult).then_inc(sg_done, 1)
                        if f:
                            high(n - 1, s, f - 1)
                        if f == 0 and not (start and q < 2):
                            dve.wait_ge(y_full, C - 1)
                        dve.wait_ge(sg_done, n + 1)
                        if not (start and q == 0 and f < 2):
                            dve.wait_ge(h_cut, n - 1)
                        nc.vector.scalar_tensor_tensor(out=h[:, f % 2, :], in0=sg[:, f % 2, :], scalar=0.5,
                                                       in1=ps_gu[f % 4][:, R:2 * R], op0=ALU.mult, op1=ALU.mult).then_inc(h_done, 1)
                        if f:
                            lower(n - 1, s, f - 1)
                    high(C * FB + FB - 1, s, FB - 1)
                    lower(C * FB + FB - 1, s, FB - 1)

            for n in range(3):
                high_weight(0, 0, n, True)
            expert(0, 0, True)
            expert(1, 1, True)
            expert(2, 0, False)
            with dve.Fori(1, E // 2 - 1) as r:
                expert(2 * r + 1, 1, False)
                expert(2 * r + 2, 0, False)
            expert(E - 1, 1, False, last=True)


def combine(nc, pl, out, scr, keep):
    TT, D = pl.TT, pl.D
    slot_from, weight = keep["slot_from"], keep["weight"]
    NBUF = 8
    with ExitStack() as ctx:
        sb = lambda name, shape, dt=F32: ctx.enter_context(nc.sbuf_tensor(name, shape, dt))
        sem = lambda name: ctx.enter_context(nc.semaphore(name))
        rows = sb("c_rows", [P, NBUF, 2, D])
        x1 = sb("c_x1", [P, NBUF, D])
        part = sb("c_part", [P, NBUF, D])
        res = sb("c_res", [P, NBUF, D])
        came = [sem(f"c_came{i}") for i in range(NBUF)]
        x1_in = [sem(f"c_x1_in{i}") for i in range(NBUF)]
        half = sem("c_half")
        summed = sem("c_summed")
        stored = [sem(f"c_stored{i}") for i in range(NBUF)]
        block = ctx.enter_context(nc.Block())

        @block.gpsimd
        def _(pool):
            for n in range(TT):
                if n >= NBUF:
                    pool.wait_ge(summed, n - NBUF + 1)
                for k in range(2):
                    pool.indirect_dma_start(out=rows[:, n % NBUF, k, :], out_offset=None, in_=scr["eout"],
                                            in_offset=bass.IndirectOffsetOnAxis(ap=slot_from[:, n, k:k + 1], axis=0)
                                            ).then_inc(came[n % NBUF], 16)

        @block.vector
        def _(dve):
            for n in range(TT):
                s = n % NBUF
                dve.wait_ge(came[s], 32 * (n // NBUF + 1))
                dve.wait_ge(x1_in[s], 16 * (n // NBUF + 1))
                nc.vector.scalar_tensor_tensor(out=part[:, s, :], in0=rows[:, s, 0, :], scalar=weight[:, n, 0:1],
                                               in1=x1[:, s, :], op0=ALU.mult, op1=ALU.add).then_inc(half, 1)
                dve.wait_ge(half, n + 1)
                if n >= NBUF:
                    dve.wait_ge(stored[s], 16 * (n // NBUF))
                nc.vector.scalar_tensor_tensor(out=res[:, s, :], in0=rows[:, s, 1, :], scalar=weight[:, n, 1:2],
                                               in1=part[:, s, :], op0=ALU.mult, op1=ALU.add).then_inc(summed, 1)

        @block.scalar
        def _(act):
            for n in range(TT):
                if n >= NBUF:
                    act.wait_ge(half, n - NBUF + 1)
                act.dma_start(x1[:, n % NBUF, :], scr["x1"][n // pl.QT, :, n % pl.QT, :]).then_inc(x1_in[n % NBUF], 16)

        @block.sync
        def _(sp):
            for n in range(TT):
                sp.wait_ge(summed, n + 1)
                sp.dma_start(out.rearrange("b (t p) d -> (b t) p d", p=P)[n], res[:, n % NBUF, :]).then_inc(stored[n % NBUF], 16)
            for s in range(NBUF):
                sp.wait_ge(stored[s], 16 * (TT // NBUF))


def build(nc, io, out):
    B, S, D = io["x"].shape
    S2 = io["ctxT"].shape[2]
    E, _, F = io["wgT"].shape
    pl = Plan(B, S, S2, D, E, F)
    dram = lambda name, shape, dt=F32: nc.dram_tensor(name, shape, dt, kind="Internal").ap()
    scr = {
        "q": dram("scr_q", (B, pl.G, 3 * pl.DK * pl.HG, S), BF16),
        "k": dram("scr_k", (B, pl.G, 3 * pl.DK * pl.HG, S2), BF16),
        "v": dram("scr_v", (B, pl.G, P, pl.KB, pl.HG * pl.VW)),
        "disp": dram("scr_disp", (E * 2 * pl.CAP, D)),
        "x1": dram("scr_x1", (B, P, pl.QT, D)),
        "eout": dram("scr_eout", (E * 2 * pl.CAP, D)),
    }
    project(nc, pl, io, scr)
    scr["q"] = scr["q"].rearrange("b g r n -> (b g) r n")
    scr["k"] = scr["k"].rearrange("b g r n -> (b g) r n")
    scr["v"] = scr["v"].rearrange("b g p k c -> (b g) p (k c)")
    with ExitStack() as ctx:
        sb = lambda name, shape, dt=F32: ctx.enter_context(nc.sbuf_tensor(name, shape, dt))
        keep = {
            "slot_to": sb("slot_to", [P, pl.TT, 2], U32),
            "slot_from": sb("slot_from", [P, pl.TT, 2], U32),
            "weight": sb("weight", [P, pl.TT, 2]),
        }
        with ExitStack() as inner:
            keep["attn"] = inner.enter_context(nc.sbuf_tensor("attn", [P, pl.ITER * pl.QT, pl.HG * pl.DK], F32))
            keep["x1"] = keep["attn"][:, :, :].rearrange("p i c -> p (i c)").rearrange("p (t d) -> p t d", d=D)
            keep["lows"] = inner.enter_context(nc.sbuf_tensor("lows", [pl.TILES, pl.ITER], F32))
            keep["nonzero"] = inner.enter_context(nc.sbuf_tensor("nonzero", [P, pl.TT], F32))
            flat = scr["disp"].rearrange("r d -> (r d)")
            scr["disp_z"] = flat.rearrange("(i p n) -> i p n", i=pl.ITER, p=P)
            attend(nc, pl, io, scr, keep)
            repair(nc, pl, io, scr, keep)
            route(nc, pl, io, scr, keep)
        R = 2 * P if (2 * pl.CAP) % (2 * P) == 0 else P
        scr["disp_c"] = scr["disp"].rearrange("(c r) d -> c r d", r=R)
        scr["eout_c"] = scr["eout"].rearrange("(c r) d -> c r d", r=R)
        experts(nc, pl, io, scr)
        combine(nc, pl, out, scr, keep)


def lay_out(inputs):
    import numpy as _np

    a = {k: _np.asarray(v) for k, v in inputs.items()}
    H, HG = 16, 4
    D = a["x"].shape[2]
    DK = D // H
    order = _np.arange(D).reshape(H // HG, HG, DK).transpose(0, 2, 1).reshape(-1)
    c = _np.ascontiguousarray
    return {
        "x": c(a["x"]),
        "ctxT": c(a["ctx_1024"].transpose(0, 2, 1)),
        "mask": c(a["mask_BxSxS2_if1"]),
        "g_xattn": c(a["g_xattn"].reshape(1, 1)),
        "g_ffn": c(a["g_ffn"].reshape(1, 1)),
        "wqT": c(a["L0_xattn_Wq"].T[:, order]),
        "wkT": c(a["L0_xattn_Wk"].T[:, order]),
        "wvT": c(a["L0_xattn_Wv"].T),
        "woT": c(a["L0_xattn_Wo"].T),
        "bq": c(a["L0_xattn_bq"][order].reshape(-1, 128).T),
        "bk": c(a["L0_xattn_bk"][order].reshape(-1, 128).T),
        "bv": c(a["L0_xattn_bv"]),
        "bo": c(a["L0_xattn_bo"]),
        "gateT": c(a["L0_ffn_gate_w"].T),
        "wgT": c(a["L0_ffn_wi_gate"].transpose(0, 2, 1)),
        "wuT": c(a["L0_ffn_wi_up"].transpose(0, 2, 1)),
        "wdT": c(a["L0_ffn_wo"].transpose(0, 2, 1)),
    }


def kernel(**inputs):
    import numpy as _np
    import concourse.bacc as _bacc
    from concourse import mybir as _mybir
    from concourse.bass_utils import run_bass_kernel_spmd as _run

    nc = _bacc.Bacc("TRN2", target_bir_lowering=False, num_devices=1)
    arrays, io = {}, {}
    for name, a in lay_out(inputs).items():
        arrays[f"in_{name}"] = a
        io[name] = nc.dram_tensor(f"in_{name}", a.shape, _mybir.dt.from_np(a.dtype), kind="ExternalInput").ap()
    shape = _np.asarray(inputs["x"]).shape
    out = nc.dram_tensor("out_0", shape, F32, kind="ExternalOutput").ap()
    build(nc, io, out)
    r = _run(nc, [arrays], core_ids=[0])
    return r.results[0]["out_0"]
```
